# Optimizing a Trainium2 kernel written in Bass

```python
import numpy as np
import jax
import jax.numpy as jnp

def _softmax(x, axis=-1):
    return jax.nn.softmax(x, axis=axis)

def _gelu(x):
    return jax.nn.gelu(x, approximate=True)

def _silu(x):
    return jax.nn.silu(x)

def _sigmoid(x):
    return jax.nn.sigmoid(x)

def _layernorm(x, axis=-1, eps=1e-05):
    m = jnp.mean(x, axis=axis, keepdims=True)
    v = jnp.var(x, axis=axis, keepdims=True)
    return (x - m) / jnp.sqrt(v + eps)

def _scatter_add(tgt, idx, src, axis=0):
    return tgt.at[idx].add(src)

def _segment_sum(src, seg, n):
    return jax.ops.segment_sum(src, seg, n)
kernel_name = 'mk_rec_standalone_d1_rec_r8_59383c'

def setup_inputs(seed: int=0):
    np.random.seed(seed)
    _w = jnp.asarray

    def _rec_inputs():
        import jax
        import jax.numpy as jnp
        _rk = jax.random.key(seed)
        r_user_feature = -0.000520686 + 1.00062 * jax.random.normal(jax.random.fold_in(_rk, 1), (2048, 128), jnp.float32)
        r_item_feature = -0.000514642 + 1.00011 * jax.random.normal(jax.random.fold_in(_rk, 2), (2048, 128), jnp.float32)
        r_user_tag = jax.random.uniform(jax.random.fold_in(_rk, 3), (2048, 512), jnp.float32, 0.0, 10)
        r_item_tag = jax.random.bernoulli(jax.random.fold_in(_rk, 4), 0.0002441, (2048, 512)).astype(jnp.float32)
        return (r_user_feature, r_item_feature, r_user_tag, r_item_tag)
    r_user_feature, r_item_feature, r_user_tag, r_item_tag = _rec_inputs()

    def _L0_rec_setup():
        import jax, jax.numpy as jnp
        import numpy as np
        B = 2048
        NUM_TAG = 512
        DIM_U = 128
        DIM_I = 128
        EPS = 1e-05

        def _batchnorm(x, gamma, beta):
            m = jnp.mean(x, axis=0)
            v = jnp.mean(jnp.square(x - m), axis=0)
            return gamma * (x - m) / jnp.sqrt(v + EPS) + beta
        key = jax.random.key(seed)
        ks = jax.random.split(key, 24)
        user_feature = jax.random.normal(ks[0], (B, DIM_U), jnp.float32)
        item_feature = jax.random.normal(ks[1], (B, DIM_I), jnp.float32)
        user_tag = jax.random.randint(ks[2], (B, NUM_TAG), 0, 11).astype(jnp.float32)
        hot = jax.random.randint(ks[3], (B,), 0, NUM_TAG)
        item_tag = jnp.zeros((B, NUM_TAG), jnp.float32).at[jnp.arange(B), hot].set(1.0)
        user_idx = jax.random.randint(ks[4], (B,), 0, 12500).astype(jnp.int32)
        item_idx = jax.random.randint(ks[5], (B,), 0, 12500).astype(jnp.int32)
        s = 0.05
        params = dict(W_user=jax.random.normal(ks[6], (10, DIM_U), jnp.float32) * s, b_user=jnp.zeros((10,), jnp.float32), W_item=jax.random.normal(ks[7], (10, DIM_I), jnp.float32) * s, b_item=jnp.zeros((10,), jnp.float32), E_user_tag=jax.random.normal(ks[8], (NUM_TAG, 5), jnp.float32), E_item_tag=jax.random.normal(ks[9], (NUM_TAG, 5), jnp.float32), g1=jnp.ones((10,), jnp.float32), be1=jnp.zeros((10,), jnp.float32), g2=jnp.ones((10,), jnp.float32), be2=jnp.zeros((10,), jnp.float32), W1=jax.random.normal(ks[10], (64, 30), jnp.float32) * s, b1=jnp.zeros((64,), jnp.float32), W2=jax.random.normal(ks[11], (32, 64), jnp.float32) * s, b2=jnp.zeros((32,), jnp.float32), W3=jax.random.normal(ks[12], (1, 32), jnp.float32) * s, b3=jnp.zeros((1,), jnp.float32))
        return dict(user_idx=user_idx, item_idx=item_idx, user_feature=user_feature, item_feature=item_feature, user_tag=user_tag, item_tag=item_tag, **params)
    _L0_rec_all = _L0_rec_setup()
    _L0_rec_in = {k: v for k, v in _L0_rec_all.items() if k in ('user_idx', 'item_idx', 'W_user', 'b_user', 'W_item', 'b_item', 'E_user_tag', 'E_item_tag', 'g1', 'be1', 'g2', 'be2', 'W1', 'b1', 'W2', 'b2', 'W3', 'b3')}
    del _L0_rec_all
    return {'r_user_feature': r_user_feature, 'r_item_feature': r_item_feature, 'r_user_tag': r_user_tag, 'r_item_tag': r_item_tag, 'L0_rec_user_idx': _L0_rec_in['user_idx'], 'L0_rec_item_idx': _L0_rec_in['item_idx'], 'L0_rec_W_user': _L0_rec_in['W_user'], 'L0_rec_b_user': _L0_rec_in['b_user'], 'L0_rec_W_item': _L0_rec_in['W_item'], 'L0_rec_b_item': _L0_rec_in['b_item'], 'L0_rec_E_user_tag': _L0_rec_in['E_user_tag'], 'L0_rec_E_item_tag': _L0_rec_in['E_item_tag'], 'L0_rec_g1': _L0_rec_in['g1'], 'L0_rec_be1': _L0_rec_in['be1'], 'L0_rec_g2': _L0_rec_in['g2'], 'L0_rec_be2': _L0_rec_in['be2'], 'L0_rec_W1': _L0_rec_in['W1'], 'L0_rec_b1': _L0_rec_in['b1'], 'L0_rec_W2': _L0_rec_in['W2'], 'L0_rec_b2': _L0_rec_in['b2'], 'L0_rec_W3': _L0_rec_in['W3'], 'L0_rec_b3': _L0_rec_in['b3']}

def reference(r_user_feature, r_item_feature, r_user_tag, r_item_tag, L0_rec_user_idx, L0_rec_item_idx, L0_rec_W_user, L0_rec_b_user, L0_rec_W_item, L0_rec_b_item, L0_rec_E_user_tag, L0_rec_E_item_tag, L0_rec_g1, L0_rec_be1, L0_rec_g2, L0_rec_be2, L0_rec_W1, L0_rec_b1, L0_rec_W2, L0_rec_b2, L0_rec_W3, L0_rec_b3):
    import jax
    import jax.numpy as jnp

    def _L0_rec_ref(user_idx, item_idx, user_feature, item_feature, user_tag, item_tag, W_user, b_user, W_item, b_item, E_user_tag, E_item_tag, g1, be1, g2, be2, W1, b1, W2, b2, W3, b3):
        import jax, jax.numpy as jnp
        import numpy as np
        B = 2048
        NUM_TAG = 512
        DIM_U = 128
        DIM_I = 128
        EPS = 1e-05

        def _batchnorm(x, gamma, beta):
            m = jnp.mean(x, axis=0)
            v = jnp.mean(jnp.square(x - m), axis=0)
            return gamma * (x - m) / jnp.sqrt(v + EPS) + beta
        user = _batchnorm(user_feature @ W_user.T + b_user, g1, be1)
        item = _batchnorm(item_feature @ W_item.T + b_item, g2, be2)
        embedd_user_tag = user_tag * 0.1 @ E_item_tag
        one_idx = jnp.argmax(item_tag == 1.0, axis=1)
        embedd_item_tag = E_user_tag[one_idx]
        feat = jnp.concatenate([user, embedd_user_tag, item, embedd_item_tag], axis=1)
        x = jax.nn.relu(feat @ W1.T + b1)
        x = jax.nn.relu(x @ W2.T + b2)
        x = jax.nn.relu(x @ W3.T + b3)
        return x
    y = _L0_rec_ref(L0_rec_user_idx, L0_rec_item_idx, r_user_feature, r_item_feature, r_user_tag, r_item_tag, L0_rec_W_user, L0_rec_b_user, L0_rec_W_item, L0_rec_b_item, L0_rec_E_user_tag, L0_rec_E_item_tag, L0_rec_g1, L0_rec_be1, L0_rec_g2, L0_rec_be2, L0_rec_W1, L0_rec_b1, L0_rec_W2, L0_rec_b2, L0_rec_W3, L0_rec_b3)
    return y

_drawn_inputs = setup_inputs


def setup_inputs(seed=0):
    import zlib

    import numpy as np

    out = dict(_drawn_inputs(seed))
    spreads = {'L0_rec_b_user': (0.0, 0.8),
     'L0_rec_b_item': (0.0, 0.8),
     'L0_rec_g1': (1.0, 0.6),
     'L0_rec_be1': (0.0, 0.8),
     'L0_rec_g2': (1.0, 0.6),
     'L0_rec_be2': (0.0, 0.535),
     'L0_rec_b1': (0.0, 0.1),
     'L0_rec_b2': (0.0, 0.1)}
    factors = {}
    for name, (base, spread) in spreads.items():
        noise = np.random.default_rng([zlib.crc32(name.encode()), seed]).standard_normal(out[name].shape)
        drawn = base * np.exp(spread * noise) if base else spread * noise
        out[name] = jnp.asarray(drawn.astype(out[name].dtype))
    for name, factor in factors.items():
        out[name] = (out[name] * factor).astype(out[name].dtype)
    return out
```

```python
from contextlib import ExitStack

import numpy as np
import concourse.bass as bass
from concourse import mybir

P = 128
F32 = mybir.dt.float32
BF16 = mybir.dt.bfloat16
FP16 = mybir.dt.float16
I32 = mybir.dt.int32
U32 = mybir.dt.uint32
ALU = mybir.AluOpType
ACT = mybir.ActivationFunctionType
AX_X = mybir.AxisListType.X

EPS = 1e-5
TAG_SCALE = 0.1

B = 2048
NTAG = 512
DU = 10
DT = 5
H1, H2 = 64, 32
G = 4
GW = P // G
C = B // (G * P)
KT = NTAG // P
HALVES = 2
TPH = B // HALVES // P
SENT = 8
ROW_USER, ROW_UTAG, ROW_ITEM, ROW_ITAG = 0, DU, DU + DT, 2 * DU + DT
NFEAT = 2 * (DU + DT)

WU = 0
WI = WU + DU
EU = WI + DU
EI = EU + KT * DT
W1 = EI + KT * DT
W2 = W1 + H1
W3 = W2 + H2
VB1, VB2, VB3 = W3 + 1, W3 + 2, W3 + 3
VBIAS, VGAM, VBET, VADD = VB3 + 1, VB3 + 2, VB3 + 3, VB3 + 4
NPACK = VADD + 1


def build(nc, user, item, utag, itag, pack, out):
    with ExitStack() as ctx:
        def sb(name, shape, dt):
            return ctx.enter_context(nc.sbuf_tensor(name, shape, dt))

        def psum(name):
            return ctx.enter_context(nc.psum_tensor(name, [P, 512], F32))

        def sem(name):
            return ctx.enter_context(nc.semaphore(name))

        par = sb("par", [P, NPACK], F32)
        feat = [sb("user_rows", [P, HALVES, TPH, P], F32), sb("item_rows", [P, HALVES, TPH, P], F32)]
        featT = [sb("userT", [P, B], F32), sb("itemT", [P, B], F32)]
        itags = sb("itags", [P, C, G, NTAG + SENT], F32)
        utags = sb("utags", [P, C, G, NTAG], F32)
        utagT = sb("utagT", [P, C, KT, G * P], F32)
        ident = sb("ident", [P, P], F32)
        ident16 = sb("ident16", [P, P], FP16)
        gfold = sb("gfold", [P, GW], F32)
        gmean = sb("gmean", [P, G, GW], F32)
        tag_id_i = sb("tag_id_i", [P, KT], I32)
        tag_id = sb("tag_id", [P, KT], F32)
        ones8 = sb("ones8", [P, 8], F32)
        w_feat = [sb("w_user", [P, GW], F32), sb("w_item", [P, GW], F32)]
        e_ut = sb("e_ut", [P, KT, GW], F32)
        e_it = sb("e_it", [P, 3, KT, GW], BF16)
        e_rest = sb("e_rest", [P, 2, KT, DT], F32)
        w1 = sb("w1", [P, 2, P], F32)
        w2 = sb("w2", [P, 2 * GW], F32)
        w3 = sb("w3", [P, G], F32)
        idx8 = sb("idx8", [P, C, G, 8], U32)
        idx16 = sb("idx16", [P, C, G], FP16)
        idxrow = sb("idxrow", [P, C, G * P], FP16)
        onehot = sb("onehot", [P, C, KT, G * P], BF16)
        stats6 = sb("stats6", [P, 6], F32)
        mv = sb("mv", [P, 2], F32)
        bn = sb("bn", [P, 12], F32)
        fin = sb("fin", [P, C, P], F32)
        h1 = sb("h1", [P, 2, P], F32)
        h2 = sb("h2", [P, P], F32)
        y = sb("y", [G, C, P], F32)

        ps_t = [psum(f"ps_t{i}") for i in range(4)]
        ps_z = psum("ps_z")
        ps_i = psum("ps_i")
        ps_m = [psum("ps_m0"), psum("ps_m1")]

        par_in = sem("par_in")
        feat_in = [[sem(f"user_in{h}") for h in range(HALVES)], [sem(f"item_in{h}") for h in range(HALVES)]]
        itag_in = [sem(f"itag_in{c}") for c in range(C)]
        utag_in = [sem(f"utag_in{c}") for c in range(C)]
        out_done = sem("out_done")
        pool_chain = sem("pool_chain")
        consts_ready = sem("consts_ready")
        weights_ready = sem("weights_ready")
        layers_ready = sem("layers_ready")
        gmean_ready = sem("gmean_ready")
        esplit_ready = sem("esplit_ready")
        turned = sem("turned")
        kept_act = sem("kept_act")
        kept_dve = sem("kept_dve")
        feat_summed = sem("feat_summed")
        mean_summed = sem("mean_summed")
        bn_done = sem("bn_done")
        std_ready = sem("std_ready")
        idx_ready = sem("idx_ready")
        idx_spread = sem("idx_spread")
        idx_kept = sem("idx_kept")
        onehot_ready = sem("onehot_ready")
        z_ready = sem("z_ready")
        fin_ready = sem("fin_ready")
        l1_done = sem("l1_done")
        h1_act = sem("h1_act")
        h1_dve = sem("h1_dve")
        l2_done = sem("l2_done")
        h2_ready = sem("h2_ready")
        l3_done = sem("l3_done")
        y_ready = sem("y_ready")

        NF = 2 * HALVES * (TPH // G)
        feat_fills = [(w, h, a) for w in range(2) for h in range(HALVES) for a in range(TPH // G)]
        fills = [("feat",) + f for f in feat_fills] + [("tag", c, k) for c in range(C) for k in range(KT)]

        def by_dve(n):
            return n < NF and n % 2 == 1

        def kept(n):
            return ((kept_dve, sum(by_dve(i) for i in range(n + 1))) if by_dve(n)
                    else (kept_act, sum(not by_dve(i) for i in range(n + 1))))

        def keep(eng_copy, n):
            src = ps_t[n % 4]
            if fills[n][0] == "feat":
                _, w, h, a = fills[n]
                dst = featT[w][:, h * (B // HALVES):(h + 1) * (B // HALVES)]
                dst = dst.rearrange("f (p t) -> f t p", t=TPH)[:, a * G:(a + 1) * G, :]
                return eng_copy(dst, src[:, :].rearrange("f (t p) -> f t p", t=G))
            _, c, k = fills[n]
            return eng_copy(utagT[:, c, k, :], src[:, :])

        block = ctx.enter_context(nc.Block())

        @block.sync
        def _(sp):
            for w, src in enumerate((user, item)):
                for h in range(HALVES):
                    rows = src[h * (B // HALVES):(h + 1) * (B // HALVES), :]
                    sp.dma_start(feat[w][:, h, :, :], rows.rearrange("(p t) d -> p t d", t=TPH)
                                 ).then_inc(feat_in[w][h], 16)

            def tags(dst, src, c, done):
                rows = src[c * G * P:(c + 1) * G * P, :]
                sp.dma_start(dst, rows.rearrange("(g p) d -> p g d", g=G)).then_inc(done, 16)

            for kind, c in (("i", 0), ("i", 1), ("u", 0), ("i", 2), ("u", 1), ("i", 3), ("u", 2), ("u", 3)):
                if kind == "i":
                    tags(itags[:, c, :, 0:NTAG], itag, c, itag_in[c])
                else:
                    tags(utags[:, c, :, :], utag, c, utag_in[c])
            for c in range(C):
                sp.wait_ge(y_ready, c + 1)
                sp.dma_start(out[c * G * P:(c + 1) * G * P, :].rearrange("(g p) o -> g (p o)", g=G),
                             y[:, c, :]).then_inc(out_done, 16)
            sp.wait_ge(out_done, 16 * C)

        @block.gpsimd
        def _(pool):
            nc.gpsimd.memset(ident[:], 0.0).then_inc(pool_chain, 1)
            nc.gpsimd.memset(ident16[:], 0.0).then_inc(pool_chain, 1)
            pool.wait_ge(pool_chain, 1)
            nc.gpsimd.affine_select(out=ident[:], in_=ident[:], compare_op=ALU.not_equal, fill=1.0, base=0,
                                    pattern=[[-1, P]], channel_multiplier=1).then_inc(consts_ready, 1)
            pool.wait_ge(pool_chain, 2)
            nc.gpsimd.affine_select(out=ident16[:], in_=ident16[:], compare_op=ALU.not_equal, fill=1.0, base=0,
                                    pattern=[[-1, P]], channel_multiplier=1).then_inc(consts_ready, 1)
            nc.gpsimd.iota(tag_id_i[:], pattern=[[P, KT]], base=0, channel_multiplier=1).then_inc(consts_ready, 1)
            nc.gpsimd.memset(ones8[:], 1.0).then_inc(consts_ready, 1)
            nc.gpsimd.memset(itags[:, :, :, NTAG:NTAG + SENT], 1.0).then_inc(consts_ready, 1)
            for t in (w_feat[0], w_feat[1], e_ut):
                last = nc.gpsimd.memset(t[:], 0.0)
            last.then_inc(pool_chain, 1)
            pool.wait_ge(pool_chain, 3)
            pool.wait_ge(par_in, 16)
            nc.gpsimd.tensor_copy(w_feat[0][:, ROW_USER:ROW_USER + DU], par[:, WU:WU + DU])
            nc.gpsimd.tensor_copy(w_feat[1][:, ROW_ITEM:ROW_ITEM + DU], par[:, WI:WI + DU])
            nc.gpsimd.tensor_copy(e_ut[:, :, ROW_UTAG:ROW_UTAG + DT],
                                  par[:, EU:EU + KT * DT].rearrange("p (k d) -> p k d", k=KT)
                                  ).then_inc(weights_ready, 1)
        @block.tensor
        def _(pe):
            def turn(n):
                if n >= 4:
                    pe.wait_ge(*kept(n - 4))
                bank = ps_t[n % 4]
                if fills[n][0] == "feat":
                    _, w, h, a = fills[n]
                    pe.wait_ge(feat_in[w][h], 16)
                    tiles = [feat[w][:, h, a * G + g, :] for g in range(G)]
                else:
                    _, c, k = fills[n]
                    pe.wait_ge(utag_in[c], 16)
                    tiles = [utags[:, c, g, k * P:(k + 1) * P] for g in range(G)]
                for g in range(G):
                    last = nc.tensor.transpose(bank[:, g * P:(g + 1) * P], tiles[g], ident[:])
                last.then_inc(turned, 1)

            def feature_products(w, half):
                for a in range(TPH // G):
                    pe.wait_ge(*kept((w * HALVES + half) * (TPH // G) + a))
                for c in range(half * C // 2, (half + 1) * C // 2):
                    for g in range(G):
                        last = nc.tensor.matmul(ps_z[g * GW:(g + 1) * GW, c * P:(c + 1) * P], w_feat[w][:],
                                                featT[w][:, (c * G + g) * P:(c * G + g + 1) * P],
                                                start=(w == 0 and c == 0), stop=False, skip_group_check=True)
                return last

            def spread_index(c):
                pe.wait_ge(idx_ready, c + 1)
                if c >= 1:
                    pe.wait_ge(idx_kept, c)
                for g in range(G):
                    last = nc.tensor.matmul(ps_i[:, g * P:(g + 1) * P], idx16[:, c, g:g + 1].to_broadcast([P, P]),
                                            ident16[:], start=True, stop=True)
                last.then_inc(idx_spread, 1)

            def tag_products(c):
                if c >= 1:
                    pe.wait_ge(fin_ready, c)
                for part in range(3):
                    for k in range(KT):
                        if part == 0:
                            pe.wait_ge(onehot_ready, c * KT + k + 1)
                        for g in range(G):
                            nc.tensor.matmul(ps_z[g * GW:(g + 1) * GW, c * P:(c + 1) * P], e_it[:, part, k, :],
                                             onehot[:, c, k, g * P:(g + 1) * P],
                                             start=False, stop=False, skip_group_check=True)
                for k in range(KT):
                    pe.wait_ge(*kept(NF + c * KT + k))
                    for g in range(G):
                        last = nc.tensor.matmul(ps_z[g * GW:(g + 1) * GW, c * P:(c + 1) * P], e_ut[:, k, :],
                                                utagT[:, c, k, g * P:(g + 1) * P], start=False,
                                                stop=(k == KT - 1), skip_group_check=True)
                last.then_inc(z_ready, 1)

            def layers(c):
                pe.wait_ge(fin_ready, c + 1)
                if c >= 1:
                    pe.wait_ge(y_ready, c)
                for a in range(2):
                    nc.tensor.matmul(ps_m[a][:, 0:P], w1[:, a, :], fin[:, c, :],
                                     start=True, stop=True).then_inc(l1_done, 1)
                for a, h1_ready in enumerate((h1_act, h1_dve)):
                    pe.wait_ge(h1_ready, c + 1)
                    last = nc.tensor.matmul(ps_m[0][a * 2 * H2:(a + 1) * 2 * H2, P:2 * P], w2[:], h1[:, a, :],
                                            start=True, stop=True)
                last.then_inc(l2_done, 1)
                pe.wait_ge(h2_ready, c + 1)
                nc.tensor.matmul(ps_m[1][0:G, P:2 * P], w3[:], h2[:], start=True, stop=True).then_inc(l3_done, 1)

            pe.wait_ge(consts_ready, 5)
            turn(0)
            turn(1)
            turn(2)
            pe.wait_ge(weights_ready, 1)
            feature_products(0, 0)
            turn(3)
            turn(4)
            feature_products(0, 1)
            turn(5)
            turn(6)
            feature_products(1, 0)
            turn(7)
            feature_products(1, 1).then_inc(feat_summed, 1)
            pe.wait_ge(gmean_ready, 1)
            pe.wait_ge(bn_done, 1)
            nc.tensor.matmul(ps_m[0][:, 0:2], gmean[:].rearrange("p g f -> p (g f)"), mv[:, 0:2],
                             start=True, stop=True).then_inc(mean_summed, 1)
            pe.wait_ge(bn_done, 2)
            nc.tensor.matmul(ps_m[1][:, 0:2], gmean[:].rearrange("p g f -> p (g f)"), bn[:, 2:4],
                             start=True, stop=True).then_inc(mean_summed, 1)
            pe.wait_ge(bn_done, 3)
            pe.wait_ge(esplit_ready, 1)
            pe.wait_ge(layers_ready, 1)
            spread_index(0)
            spread_index(1)
            for c in range(C):
                for k in range(KT):
                    turn(NF + c * KT + k)
                tag_products(c)
                layers(c)
                if c + 2 < C:
                    spread_index(c + 2)

        @block.scalar
        def _(act):
            act.dma_start(par[:], pack).then_inc(par_in, 16)

            def keep_fill(n):
                act.wait_ge(turned, n + 1)
                keep(nc.scalar.copy, n).then_inc(kept_act, 1)

            for n in range(0, NF, 2):
                keep_fill(n)
            act.wait_ge(mean_summed, 2)
            act.wait_ge(bn_done, 3)
            nc.scalar.activation(bn[:, 7:8], bn[:, 6:7], ACT.Sqrt).then_inc(std_ready, 1)

            def keep_index(c):
                act.wait_ge(idx_spread, c + 1)
                nc.scalar.copy(idxrow[:, c, :], ps_i[:, :]).then_inc(idx_kept, 1)

            keep_index(0)
            keep_index(1)
            for c in range(C):
                for k in range(KT):
                    keep_fill(NF + c * KT + k)
                act.wait_ge(l1_done, 2 * c + 1)
                nc.scalar.activation(h1[:, 0, :], ps_m[0][:, 0:P], ACT.Relu,
                                     bias=par[:, VB1:VB1 + 1]).then_inc(h1_act, 1)
                act.wait_ge(l2_done, c + 1)
                nc.scalar.activation(h2[:], ps_m[0][:, P:2 * P], ACT.Relu,
                                     bias=par[:, VB2:VB2 + 1]).then_inc(h2_ready, 1)
                act.wait_ge(l3_done, c + 1)
                nc.scalar.activation(y[:, c, :], ps_m[1][0:G, P:2 * P], ACT.Relu,
                                     bias=par[0:G, VB3:VB3 + 1]).then_inc(y_ready, 1)
                if c + 2 < C:
                    keep_index(c + 2)

        @block.vector
        def _(dve):
            chain = sem("dve_chain")
            count = [0]

            def link(ins):
                count[0] += 1
                ins.then_inc(chain, 1)
                dve.wait_ge(chain, count[0])

            link(nc.vector.memset(e_it[:], 0.0))
            dve.wait_ge(par_in, 16)
            e = par[:, EI:EI + KT * DT].rearrange("p (k d) -> p k d", k=KT)
            part = [e_it[:, i, :, ROW_ITAG:ROW_ITAG + DT] for i in range(3)]
            link(nc.vector.tensor_copy(part[0], e))
            link(nc.vector.tensor_tensor(e_rest[:, 0], e, part[0], ALU.subtract))
            link(nc.vector.tensor_copy(part[1], e_rest[:, 0]))
            link(nc.vector.tensor_tensor(e_rest[:, 1], e_rest[:, 0], part[1], ALU.subtract))
            nc.vector.tensor_copy(part[2], e_rest[:, 1]).then_inc(esplit_ready, 1)
            for t in (w1, w2, w3):
                last = nc.vector.memset(t[:], 0.0)
            link(last)
            for g in range(G):
                q = slice(g * GW, (g + 1) * GW)
                nc.vector.tensor_copy(w1[q, g // 2, (g % 2) * H1:(g % 2 + 1) * H1], par[q, W1:W1 + H1])
                nc.vector.tensor_copy(w3[q, g:g + 1], par[q, W3:W3 + 1])
            for a in range(2):
                q = slice(a * H1, (a + 1) * H1)
                last = nc.vector.tensor_copy(w2[q, a * H2:(a + 1) * H2], par[q, W2:W2 + H2])
            last.then_inc(layers_ready, 1)
            dve.wait_ge(consts_ready, 5)
            link(nc.vector.tensor_copy(tag_id[:], tag_id_i[:]))
            link(nc.vector.tensor_reduce(gfold[:], ident[:].rearrange("p (g f) -> p f g", g=G), AX_X, ALU.add))
            for g in range(G):
                last = nc.vector.tensor_scalar(gmean[:, g, :], gfold[:], 1.0 / G, None, ALU.mult)
            last.then_inc(gmean_ready, 1)

            for n in range(1, NF, 2):
                dve.wait_ge(turned, n + 1)
                keep(nc.vector.tensor_copy, n).then_inc(kept_dve, 1)

            dve.wait_ge(feat_summed, 1)
            link(nc.vector.bn_stats(stats6[:], ps_z[:, :]))
            nc.vector.bn_aggr(mv[:], stats6[:]).then_inc(bn_done, 1)
            dve.wait_ge(mean_summed, 1)
            mean, dev, var_g, scale, shift = (bn[:, i:i + 1] for i in (0, 1, 2, 4, 5))
            link(nc.vector.tensor_copy(mean, ps_m[0][:, 0:1]))
            link(nc.vector.tensor_tensor(dev, mv[:, 0:1], mean, ALU.subtract))
            link(nc.vector.tensor_copy(bn[:, 3:4], dev))
            nc.vector.scalar_tensor_tensor(out=var_g, in0=dev, scalar=dev, in1=mv[:, 1:2],
                                           op0=ALU.mult, op1=ALU.add).then_inc(bn_done, 1)
            dve.wait_ge(mean_summed, 2)
            nc.vector.tensor_scalar(bn[:, 6:7], ps_m[1][:, 0:1], EPS, None, ALU.add).then_inc(bn_done, 1)
            link(nc.vector.tensor_tensor(bn[:, 8:9], mean, par[:, VBIAS:VBIAS + 1], ALU.add))
            link(nc.vector.tensor_tensor(bn[:, 9:10], par[:, VBIAS:VBIAS + 1], bn[:, 8:9], ALU.subtract))
            dve.wait_ge(std_ready, 1)
            link(nc.vector.reciprocal(bn[:, 10:11], bn[:, 7:8]))
            link(nc.vector.tensor_tensor(bn[:, 11:12], bn[:, 10:11], par[:, VGAM:VGAM + 1], ALU.mult))
            link(nc.vector.scalar_tensor_tensor(out=shift, in0=bn[:, 9:10], scalar=bn[:, 11:12],
                                                in1=par[:, VBET:VBET + 1], op0=ALU.mult, op1=ALU.add))
            link(nc.vector.tensor_tensor(scale, bn[:, 11:12], par[:, VADD:VADD + 1], ALU.add))

            def find_index(c):
                dve.wait_ge(itag_in[c], 16)
                for g in range(G):
                    last = nc.vector.max_index(idx8[:, c, g, :], ones8[:], itags[:, c, g, :])
                link(last)
                nc.vector.scalar_tensor_tensor(out=idx16[:, c, :], in0=idx8[:, c, :, 0], scalar=float(NTAG),
                                               in1=idx8[:, c, :, 0], op0=ALU.is_lt,
                                               op1=ALU.mult).then_inc(idx_ready, 1)

            def one_hot(c):
                dve.wait_ge(idx_kept, c + 1)
                for k in range(KT):
                    nc.vector.tensor_scalar(onehot[:, c, k, :], idxrow[:, c, :], tag_id[:, k:k + 1], None,
                                            ALU.is_equal).then_inc(onehot_ready, 1)

            def layers(c):
                dve.wait_ge(z_ready, c + 1)
                nc.vector.tensor_scalar(fin[:, c, :], ps_z[:, c * P:(c + 1) * P], scale, shift,
                                        ALU.mult, ALU.add).then_inc(fin_ready, 1)
                dve.wait_ge(l1_done, 2 * c + 2)
                nc.vector.tensor_scalar(h1[:, 1, :], ps_m[1][:, 0:P], par[:, VB1:VB1 + 1], 0.0,
                                        ALU.add, ALU.max).then_inc(h1_dve, 1)

            find_index(0)
            one_hot(0)
            find_index(1)
            one_hot(1)
            for c in range(C):
                layers(c)
                if c + 2 < C:
                    find_index(c + 2)
                    one_hot(c + 2)


def _pack(i):
    p = np.zeros((P, NPACK), np.float32)
    p[:, WU:WU + DU] = i["L0_rec_W_user"].T
    p[:, WI:WI + DU] = i["L0_rec_W_item"].T
    for k in range(KT):
        p[:, EU + k * DT:EU + (k + 1) * DT] = i["L0_rec_E_item_tag"][k * P:(k + 1) * P]
        p[:, EI + k * DT:EI + (k + 1) * DT] = i["L0_rec_E_user_tag"][k * P:(k + 1) * P]
    for g in range(G):
        o = g * GW
        p[o:o + NFEAT, W1:W1 + H1] = i["L0_rec_W1"].T
        p[o:o + H2, W3:W3 + 1] = i["L0_rec_W3"].T
        p[o:o + H2, VB2] = i["L0_rec_b2"]
        for row, b, gam, bet in ((ROW_USER, "b_user", "g1", "be1"), (ROW_ITEM, "b_item", "g2", "be2")):
            p[o + row:o + row + DU, VBIAS] = i["L0_rec_" + b]
            p[o + row:o + row + DU, VGAM] = i["L0_rec_" + gam]
            p[o + row:o + row + DU, VBET] = i["L0_rec_" + bet]
        p[o + ROW_UTAG:o + ROW_UTAG + DT, VADD] = TAG_SCALE
        p[o + ROW_ITAG:o + ROW_ITAG + DT, VADD] = 1.0
    for a in range(2):
        p[a * H1:(a + 1) * H1, W2:W2 + H2] = i["L0_rec_W2"].T
        p[a * H1:(a + 1) * H1, VB1] = i["L0_rec_b1"]
    p[:, VB3] = i["L0_rec_b3"][0]
    return p


def kernel(**inputs):
    import concourse.bacc as _bacc
    from concourse.bass_utils import run_bass_kernel_spmd as _run

    i = {k: np.asarray(v) for k, v in inputs.items()}
    arrays = {
        "user": np.ascontiguousarray(i["r_user_feature"]),
        "item": np.ascontiguousarray(i["r_item_feature"]),
        "utag": np.ascontiguousarray(i["r_user_tag"]),
        "itag": np.ascontiguousarray(i["r_item_tag"]),
        "pack": _pack(i),
    }
    nc = _bacc.Bacc("TRN2", target_bir_lowering=False, num_devices=1)
    args = [nc.dram_tensor(n, a.shape, F32, kind="ExternalInput").ap() for n, a in arrays.items()]
    out = nc.dram_tensor("out", (B, 1), F32, kind="ExternalOutput").ap()
    build(nc, *args, out)
    r = _run(nc, [arrays], core_ids=[0])
    return r.results[0]["out"]
```

```python
from contextlib import ExitStack

import numpy as np
import concourse.bass as bass
from concourse import mybir

P = 128
F32 = mybir.dt.float32
BF16 = mybir.dt.bfloat16
FP16 = mybir.dt.float16
I32 = mybir.dt.int32
U32 = mybir.dt.uint32
ALU = mybir.AluOpType
ACT = mybir.ActivationFunctionType
AX_X = mybir.AxisListType.X

EPS = 1e-5
TAG_SCALE = 0.1

B = 2048
NTAG = 512
DU = 10
DT = 5
H1, H2 = 64, 32
G = 4
GW = P // G
C = B // (G * P)
KT = NTAG // P
HALVES = 2
TPH = B // HALVES // P
SENT = 8
ROW_USER, ROW_UTAG, ROW_ITEM, ROW_ITAG = 0, DU, DU + DT, 2 * DU + DT
WARM = 6
NFEAT = 2 * (DU + DT)

WU = 0
WI = WU + DU
EU = WI + DU
EI = EU + KT * DT
W1 = EI + KT * DT
W2 = W1 + H1
W3 = W2 + H2
VB1, VB2, VB3 = W3 + 1, W3 + 2, W3 + 3
VBIAS, VGAM, VBET, VADD = VB3 + 1, VB3 + 2, VB3 + 3, VB3 + 4
VBLK = VADD + 1
NPACK = VBLK + 1


def utag_pieces(c):
    return [(0, 2), (2, 3), (3, 4)] if c == C - 1 else [(0, 2), (2, 4)]


def build(nc, user, item, utag, itag, pack, out):
    fills = [("feat", w, h, a) for w in range(2) for h in range(HALVES) for a in range(TPH // G)]
    copier = ["act", "dve"] * (len(fills) // 2)
    ALL = range(G)
    for what in ((0, 0), (0, 1), "index 0", (0, 2), (0, 3), (1, 0), (1, 1), "index 1", (1, 2), (1, 3),
                 (2, 0), (2, 1), "index 2", (2, 2), (2, 3), (3, 0), "index 3", (3, 1), (3, 2)):
        if isinstance(what, str):
            fills.append(("index", int(what[-1])))
            copier.append("dve")
        else:
            fills.append(("tag",) + what + (ALL,))
            copier.append("act")
    fills += [("tag", C - 1, KT - 1, range(0, G // 2)), ("tag", C - 1, KT - 1, range(G // 2, G))]
    copier += ["act", "dve"]

    with ExitStack() as ctx:
        def sb(name, shape, dt):
            return ctx.enter_context(nc.sbuf_tensor(name, shape, dt))

        def psum(name):
            return ctx.enter_context(nc.psum_tensor(name, [P, 512], F32))

        def sem(name):
            return ctx.enter_context(nc.semaphore(name))

        par = sb("par", [P, NPACK], F32)
        feat = [sb("user_rows", [P, HALVES, TPH, P], F32), sb("item_rows", [P, HALVES, TPH, P], F32)]
        featT = [sb("userT", [P, B], F32), sb("itemT", [P, B], F32)]
        itags = sb("itags", [P, C, G, NTAG + SENT], F32)
        utags = sb("utags", [P, C, G, NTAG], F32)
        utagT = sb("utagT", [P, C, KT, G * P], F32)
        ident = sb("ident", [P, P], F32)
        ident16 = sb("ident16", [P, P], FP16)
        gfold = sb("gfold", [P, GW], F32)
        gmean = sb("gmean", [P, G, GW], F32)
        row_i = sb("row_i", [P, 1], I32)
        row = sb("row", [P, 1], F32)
        ones8 = sb("ones8", [P, 8], F32)
        w_feat = [sb("w_user", [P, GW], F32), sb("w_item", [P, GW], F32)]
        e_ut = sb("e_ut", [P, KT, GW], F32)
        e_it = sb("e_it", [P, 3, GW], BF16)
        e_rest = sb("e_rest", [P, 2, KT * DT], F32)
        pick = sb("pick", [P, G, GW], F32)
        w1 = sb("w1", [P, 2, P], F32)
        w2 = sb("w2", [P, 2 * GW], F32)
        w3 = sb("w3", [P, G], F32)
        idx8 = sb("idx8", [P, C, G, 8], U32)
        lohi = sb("lohi", [P, 2, C, G], U32)
        lohi16 = sb("lohi16", [P, 2, C, G], FP16)
        onehot = sb("onehot", [P, C, G * P], BF16)
        mask = sb("mask", [P, C, P], F32)
        looked = sb("looked", [P, C, P], F32)
        stats6 = sb("stats6", [P, 2, 6], F32)
        mv = sb("mv", [P, 2], F32)
        mean_bias = sb("mean_bias", [P, 1], F32)
        dev = sb("dev", [P, 1], F32)
        dev2 = sb("dev2", [P, 1], F32)
        less_mean = sb("less_mean", [P, 1], F32)
        eps = sb("eps", [P, 1], F32)
        std = sb("std", [P, 1], F32)
        rstd = sb("rstd", [P, 1], F32)
        gain = sb("gain", [P, 1], F32)
        scale = sb("scale", [P, 1], F32)
        shift = sb("shift", [P, 1], F32)
        fin = sb("fin", [P, C, P], F32)
        h1 = sb("h1", [P, 2, 2, P], F32)
        h2 = sb("h2", [P, 2, P], F32)
        y = sb("y", [G, C, P], F32)

        ps_t = [psum(f"ps_t{i}") for i in range(4)]
        ps_z = [psum("ps_z0"), psum("ps_z1")]
        ps_x = psum("ps_x")
        ps_m = psum("ps_m")

        par_in = sem("par_in")
        feat_in = [[sem(f"user_in{h}") for h in range(HALVES)], [sem(f"item_in{h}") for h in range(HALVES)]]
        itag_in = [[sem(f"itag_in{c}_{h}") for h in range(2)] for c in range(C)]
        utag_in = [[sem(f"utag_in{c}_{k}") for k, _ in utag_pieces(c)] for c in range(C)]
        ident_ready = sem("ident_ready")
        out_done = sem("out_done")
        pool_chain = sem("pool_chain")
        consts_ready = sem("consts_ready")
        weights_ready = sem("weights_ready")
        layers_ready = sem("layers_ready")
        gmean_ready = sem("gmean_ready")
        esplit_ready = sem("esplit_ready")
        turned = sem("turned")
        kept_act = sem("kept_act")
        kept_dve = sem("kept_dve")
        feat_summed = sem("feat_summed")
        mean_summed = sem("mean_summed")
        var_summed = sem("var_summed")
        eps_ready = sem("eps_ready")
        bn_done = sem("bn_done")
        std_ready = sem("std_ready")
        table_in = sem("table_in")
        factors_ready = sem("factors_ready")
        idx_ready = sem("idx_ready")
        mask_ready = sem("mask_ready")
        block_rows = sem("block_rows")
        looked_ready = sem("looked_ready")
        z_ready = sem("z_ready")
        fin_ready = sem("fin_ready")
        l1_done = sem("l1_done")
        h1_act = sem("h1_act")
        h1_dve = sem("h1_dve")
        l2_done = sem("l2_done")
        h2_ready = [sem(f"h2_ready{c}") for c in range(C)]
        l3_done = sem("l3_done")
        y_ready = [sem(f"y_ready{c}") for c in range(C)]

        def kept(n):
            return {"act": kept_act, "dve": kept_dve}[copier[n]], copier[:n + 1].count(copier[n])

        def keep(eng_copy, n):
            src = ps_t[n % 4]
            if fills[n][0] == "feat":
                _, w, h, a = fills[n]
                dst = featT[w][:, h * (B // HALVES):(h + 1) * (B // HALVES)]
                dst = dst.rearrange("f (p t) -> f t p", t=TPH)[:, a * G:(a + 1) * G, :]
                return eng_copy(dst, src[:, :].rearrange("f (t p) -> f t p", t=G))
            _, c, k, groups = fills[n]
            cols = slice(groups.start * P, groups.stop * P)
            return eng_copy(utagT[:, c, k, cols], src[:, cols])

        layer_fill = fills.index(("tag", C - 1, 1, ALL))
        ps_layer = ps_t[layer_fill % 4]
        def l1_of(c, a):
            if c == C - 1 and a == 1:
                return ps_x[:, 2 * P:3 * P]
            bank = ps_layer if c == C - 2 else ps_m
            return bank[:, a * P:(a + 1) * P]

        def l2_of(c):
            return ps_z[0][:, 0:P] if c == C - 2 else ps_m[:, 2 * P:3 * P]

        def l3_of(c):
            return ps_z[0][0:G, P:2 * P] if c == C - 2 else ps_m[0:G, 3 * P:4 * P]

        def h1_ready(c):
            return (h1_dve, 1) if c == C - 2 else (h1_act, min(c + 1, C - 1))

        block = ctx.enter_context(nc.Block())

        @block.sync
        def _(sp):
            sp.dma_start(par[:], pack).then_inc(par_in, 16)
            for w, src in enumerate((user, item)):
                for h in range(HALVES):
                    rows = src[h * (B // HALVES):(h + 1) * (B // HALVES), :]
                    sp.dma_start(feat[w][:, h, :, :], rows.rearrange("(p t) d -> p t d", t=TPH)
                                 ).then_inc(feat_in[w][h], 16)

            for kind, c in (("i", 0), ("u", 0), ("i", 1), ("u", 1), ("i", 2), ("u", 2), ("i", 3), ("u", 3)):
                rows = slice(c * G * P, (c + 1) * G * P)
                if kind == "i":
                    src = itag[rows, :].rearrange("(g p) d -> p g d", g=G)
                    for h in range(2):
                        gs = slice(h * G // 2, (h + 1) * G // 2)
                        sp.dma_start(itags[:, c, gs, 0:NTAG], src[:, gs, :]).then_inc(itag_in[c][h], 16)
                else:
                    src = utag[rows, :].rearrange("(g p) d -> p g d", g=G)
                    for i, (k0, k1) in enumerate(utag_pieces(c)):
                        ds = slice(k0 * P, k1 * P)
                        sp.dma_start(utags[:, c, :, ds], src[:, :, ds]).then_inc(utag_in[c][i], 16)
            for c in range(C):
                sp.wait_ge(y_ready[c], 1)
                sp.dma_start(out[c * G * P:(c + 1) * G * P, :].rearrange("(g p) o -> g (p o)", g=G),
                             y[:, c, :]).then_inc(out_done, 16)
            sp.wait_ge(out_done, 16 * C)

        @block.gpsimd
        def _(pool):
            nc.gpsimd.memset(ident[:], 0.0).then_inc(pool_chain, 1)
            nc.gpsimd.memset(ident16[:], 0.0).then_inc(pool_chain, 1)
            pool.wait_ge(pool_chain, 1)
            nc.gpsimd.affine_select(out=ident[:], in_=ident[:], compare_op=ALU.not_equal, fill=1.0, base=0,
                                    pattern=[[-1, P]], channel_multiplier=1).then_inc(ident_ready, 1)
            pool.wait_ge(pool_chain, 2)
            nc.gpsimd.affine_select(out=ident16[:], in_=ident16[:], compare_op=ALU.not_equal, fill=1.0, base=0,
                                    pattern=[[-1, P]], channel_multiplier=1).then_inc(consts_ready, 1)
            nc.gpsimd.iota(row_i[:], pattern=[[0, 1]], base=0, channel_multiplier=1).then_inc(consts_ready, 1)
            nc.gpsimd.memset(ones8[:], 1.0).then_inc(consts_ready, 1)
            nc.gpsimd.memset(itags[:, :, :, NTAG:NTAG + SENT], 1.0).then_inc(consts_ready, 1)
            for t in (w_feat[0], w_feat[1], e_ut):
                last = nc.gpsimd.memset(t[:], 0.0)
            last.then_inc(pool_chain, 1)
            pool.wait_ge(pool_chain, 3)
            pool.wait_ge(par_in, 16)
            nc.gpsimd.tensor_copy(w_feat[0][:, ROW_USER:ROW_USER + DU], par[:, WU:WU + DU])
            nc.gpsimd.tensor_copy(w_feat[1][:, ROW_ITEM:ROW_ITEM + DU], par[:, WI:WI + DU])
            nc.gpsimd.tensor_copy(e_ut[:, :, ROW_UTAG:ROW_UTAG + DT],
                                  par[:, EU:EU + KT * DT].rearrange("p (k d) -> p k d", k=KT)
                                  ).then_inc(weights_ready, 1)

        @block.tensor
        def _(pe):
            def turn(n):
                if n >= 4:
                    pe.wait_ge(*kept(n - 4))
                bank = ps_t[n % 4]
                if fills[n][0] == "feat":
                    _, w, h, a = fills[n]
                    pe.wait_ge(feat_in[w][h], 16)
                    for g in range(G):
                        last = nc.tensor.transpose(bank[:, g * P:(g + 1) * P], feat[w][:, h, a * G + g, :], ident[:])
                elif fills[n][0] == "index":
                    _, c = fills[n]
                    pe.wait_ge(idx_ready, c + 1)
                    if c >= 1:
                        pe.wait_ge(looked_ready, c)
                    for g in range(G):
                        nc.tensor.matmul(ps_x[g * GW:(g + 1) * GW, 0:P], lohi16[:, 1, c, g:g + 1].to_broadcast([P, GW]),
                                         ident16[:], start=True, stop=True)
                    for g in range(G):
                        last = nc.tensor.matmul(bank[:, g * P:(g + 1) * P],
                                                lohi16[:, 0, c, g:g + 1].to_broadcast([P, P]),
                                                ident16[:], start=True, stop=True)
                else:
                    _, c, k, groups = fills[n]
                    pe.wait_ge(utag_in[c][[k0 <= k < k1 for k0, k1 in utag_pieces(c)].index(True)], 16)
                    for g in groups:
                        last = nc.tensor.transpose(bank[:, g * P:(g + 1) * P], utags[:, c, g, k * P:(k + 1) * P],
                                                   ident[:])
                last.then_inc(turned, 1)

            def z_of(c, g):
                return ps_z[c % 2][g * GW:(g + 1) * GW, (c // 2) * P:(c // 2 + 1) * P]

            def feature_products(w, half):
                for a in range(TPH // G):
                    pe.wait_ge(*kept((w * HALVES + half) * (TPH // G) + a))
                for c in range(half * C // 2, (half + 1) * C // 2):
                    for g in range(G):
                        last = nc.tensor.matmul(z_of(c, g), w_feat[w][:],
                                                featT[w][:, (c * G + g) * P:(c * G + g + 1) * P],
                                                start=(w == 0 and c < 2), stop=False, skip_group_check=True)
                return last

            def look_up(c):
                pe.wait_ge(*kept(fills.index(("index", c))))
                for part in range(3):
                    for g in range(G):
                        last = nc.tensor.matmul(ps_x[g * GW:(g + 1) * GW, P:2 * P], e_it[:, part, :],
                                                onehot[:, c, g * P:(g + 1) * P],
                                                start=(part == 0), stop=(part == 2))
                last.then_inc(block_rows, 1)

            def pick_block(c, last=False):
                pe.wait_ge(looked_ready, c + 1)
                if c >= 2:
                    pe.wait_ge(fin_ready, c - 1)
                mm = nc.tensor.matmul(ps_z[c % 2][:, (c // 2) * P:(c // 2 + 1) * P],
                                      pick[:].rearrange("p g f -> p (g f)"), looked[:, c, :],
                                      start=False, stop=last, skip_group_check=True)
                if last:
                    mm.then_inc(z_ready, 1)

            def tag_products(c, block=None, last=False):
                if c >= 2:
                    pe.wait_ge(fin_ready, c - 1)
                for n, what in enumerate(fills):
                    if what[:2] != ("tag", c) or block not in (None, what[2]):
                        continue
                    _, _, k, groups = what
                    pe.wait_ge(*kept(n))
                    for g in groups:
                        mm = nc.tensor.matmul(z_of(c, g), e_ut[:, k, :], utagT[:, c, k, g * P:(g + 1) * P],
                                              start=False, stop=(last and k == KT - 1), skip_group_check=True)
                if last:
                    mm.then_inc(z_ready, 1)

            def layer1(c):
                pe.wait_ge(fin_ready, c + 1)
                if c == C - 2:
                    pe.wait_ge(*kept(layer_fill))
                elif c >= 1:
                    pe.wait_ge(y_ready[min(c, C - 2) - 1], 1)
                if c == C - 1:
                    pe.wait_ge(looked_ready, C)
                for a in range(2):
                    last = nc.tensor.matmul(l1_of(c, a), w1[:, a, :], fin[:, c, :], start=True, stop=True)
                    if a == 0 and c == C - 1:
                        last.then_inc(l1_done, 1)
                last.then_inc(l1_done, 1)

            def layer2(c):
                pe.wait_ge(*h1_ready(c))
                if c == C - 2:
                    pe.wait_ge(fin_ready, c + 1)
                for a in range(2):
                    if a == 1 and c == C - 1:
                        pe.wait_ge(h1_dve, 2)
                    last = nc.tensor.matmul(l2_of(c)[a * 2 * H2:(a + 1) * 2 * H2, :], w2[:], h1[:, c % 2, a, :],
                                            start=True, stop=True)
                last.then_inc(l2_done, 1)

            def layer3(c):
                pe.wait_ge(h2_ready[c], 1)
                nc.tensor.matmul(l3_of(c), w3[:], h2[:, c % 2, :], start=True, stop=True).then_inc(l3_done, 1)

            at = [0]

            def turns(count):
                for n in range(at[0], at[0] + count):
                    turn(n)
                at[0] += count

            pe.wait_ge(ident_ready, 1)
            for _ in range(WARM):
                nc.tensor.matmul(ps_m[:, 0:P], ident[:], ident[:], start=True, stop=True)
            turns(5)
            pe.wait_ge(weights_ready, 1)
            feature_products(0, 0)
            turns(1)
            feature_products(0, 1)
            turns(2)
            feature_products(1, 0)
            feature_products(1, 1).then_inc(feat_summed, 1)
            turns(1)
            pe.wait_ge(gmean_ready, 1)
            pe.wait_ge(bn_done, 1)
            over_groups = gmean[:].rearrange("p g f -> p (g f)")
            nc.tensor.matmul(ps_m[:, 0:1], over_groups, mv[:, 0:1], start=True, stop=True).then_inc(mean_summed, 1)
            turns(1)
            pe.wait_ge(consts_ready, 4)
            turns(1)
            pe.wait_ge(bn_done, 3)
            nc.tensor.matmul(ps_m[:, 0:1], over_groups, dev2[:, 0:1], start=True, stop=True).then_inc(var_summed, 1)
            turns(2)
            pe.wait_ge(esplit_ready, 1)
            look_up(0)
            tag_products(0)
            pe.wait_ge(layers_ready, 1)
            pick_block(0, last=True)
            pe.wait_ge(std_ready, 1)
            turns(1)
            layer1(0)
            turns(2)
            layer2(0)
            turns(1)
            layer3(0)
            turns(1)
            look_up(1)
            tag_products(1)
            pick_block(1, last=True)
            turns(1)
            layer1(1)
            turns(2)
            layer2(1)
            turns(1)
            layer3(1)
            turns(1)
            look_up(2)
            tag_products(2)
            pick_block(2, last=True)
            turns(4)
            tag_products(3, 0)
            look_up(3)
            turns(2)
            tag_products(3, 1)
            tag_products(3, 2)
            pick_block(3)
            tag_products(3, 3, last=True)
            layer1(2)
            layer1(3)
            layer2(2)
            layer2(3)
            layer3(2)
            layer3(3)

        @block.scalar
        def _(act):
            act.wait_ge(eps_ready, 1)
            nc.scalar.activation(std[:], eps[:], ACT.Sqrt).then_inc(table_in, 1)

            def keeps(*what):
                for n, f in enumerate(fills):
                    if copier[n] == "act" and f[:len(what)] == what:
                        act.wait_ge(turned, n + 1)
                        keep(nc.scalar.copy, n).then_inc(kept_act, 1)

            def features(c):
                act.wait_ge(factors_ready, 2)
                act.wait_ge(z_ready, c + 1)
                nc.scalar.activation(fin[:, c, :], ps_z[c % 2][:, (c // 2) * P:(c // 2 + 1) * P], ACT.Identity,
                                     bias=shift[:], scale=scale[:]).then_inc(fin_ready, 1)

            def hidden1(c):
                both = 1 if c == C - 1 else 2
                act.wait_ge(l1_done, c + 1)
                if c == C - 1:
                    act.wait_ge(l2_done, c - 1)
                nc.scalar.activation(h1[:, c % 2, 0:both, :].rearrange("p a n -> p (a n)"), ps_m[:, 0:both * P],
                                     ACT.Relu, bias=par[:, VB1:VB1 + 1]).then_inc(h1_act, 1)

            def hidden2(c):
                act.wait_ge(l2_done, c + 1)
                if c == C - 1:
                    act.wait_ge(l3_done, c - 1)
                nc.scalar.activation(h2[:, c % 2, :], l2_of(c), ACT.Relu,
                                     bias=par[:, VB2:VB2 + 1]).then_inc(h2_ready[c], 1)

            def output(c):
                act.wait_ge(l3_done, c + 1)
                nc.scalar.activation(y[:, c, :], l3_of(c), ACT.Relu,
                                     bias=par[0:G, VB3:VB3 + 1]).then_inc(y_ready[c], 1)

            keeps("feat")
            keeps("tag", 0, 0)
            keeps("tag", 0, 1)
            act.wait_ge(var_summed, 1)
            act.wait_ge(table_in, 1)
            nc.scalar.activation(std[:], ps_m[:, 0:1], ACT.Sqrt, bias=eps[:]).then_inc(std_ready, 1)
            keeps("tag", 0, 2)
            keeps("tag", 0, 3)
            features(0)
            keeps("tag", 1, 0)
            hidden1(0)
            keeps("tag", 1, 1)
            hidden2(0)
            keeps("tag", 1, 2)
            output(0)
            keeps("tag", 1, 3)
            features(1)
            keeps("tag", 2, 0)
            hidden1(1)
            keeps("tag", 2, 1)
            hidden2(1)
            keeps("tag", 2, 2)
            output(1)
            keeps("tag", 2, 3)
            features(2)
            keeps("tag", 3, 0)
            keeps("tag", 3, 1)
            keeps("tag", 3, 2)
            keeps("tag", 3, 3)
            for step in (features, hidden1, hidden2, output):
                step(3)

        @block.vector
        def _(dve):
            chain = sem("dve_chain")
            count = [0]

            def link(ins):
                count[0] += 1
                ins.then_inc(chain, 1)
                dve.wait_ge(chain, count[0])

            nc.vector.memset(eps[:], EPS).then_inc(eps_ready, 1)
            link(nc.vector.memset(e_it[:], 0.0))
            dve.wait_ge(par_in, 16)
            e = par[:, EI:EI + KT * DT]
            part = [e_it[:, i, 0:KT * DT] for i in range(3)]
            link(nc.vector.tensor_copy(part[0], e))
            link(nc.vector.tensor_tensor(e_rest[:, 0], e, part[0], ALU.subtract))
            link(nc.vector.tensor_copy(part[1], e_rest[:, 0]))
            link(nc.vector.tensor_tensor(e_rest[:, 1], e_rest[:, 0], part[1], ALU.subtract))
            nc.vector.tensor_copy(part[2], e_rest[:, 1]).then_inc(esplit_ready, 1)
            for t in (w1, w2, w3, pick):
                last = nc.vector.memset(t[:], 0.0)
            link(last)
            for g in range(G):
                q = slice(g * GW, (g + 1) * GW)
                nc.vector.tensor_copy(w1[q, g // 2, (g % 2) * H1:(g % 2 + 1) * H1], par[q, W1:W1 + H1])
                nc.vector.tensor_copy(w3[q, g:g + 1], par[q, W3:W3 + 1])
            for a in range(2):
                q = slice(a * H1, (a + 1) * H1)
                nc.vector.tensor_copy(w2[q, a * H2:(a + 1) * H2], par[q, W2:W2 + H2])
            dve.wait_ge(ident_ready, 1)
            blocks = ident[:].rearrange("p (g f) -> p g f", g=G)[:, :, 0:KT * DT]
            nc.vector.tensor_reduce(pick[:, :, ROW_ITAG:ROW_ITAG + DT], blocks.rearrange("p g (k d) -> p g d k", k=KT),
                                    AX_X, ALU.add).then_inc(layers_ready, 1)
            dve.wait_ge(consts_ready, 4)
            link(nc.vector.tensor_copy(row[:], row_i[:]))
            link(nc.vector.tensor_reduce(gfold[:], ident[:].rearrange("p (g f) -> p f g", g=G), AX_X, ALU.add))
            for g in range(G):
                last = nc.vector.tensor_scalar(gmean[:, g, :], gfold[:], 1.0 / G, None, ALU.mult)
            last.then_inc(gmean_ready, 1)

            def keeps(*what):
                for n, f in enumerate(fills):
                    if copier[n] == "dve" and f[:len(what)] == what:
                        dve.wait_ge(turned, n + 1)
                        keep(nc.vector.tensor_copy, n).then_inc(kept_dve, 1)

            def group_statistics():
                dve.wait_ge(feat_summed, 1)
                nc.vector.bn_stats(stats6[:, 0, :], ps_z[0][:, 0:2 * P])
                link(nc.vector.bn_stats(stats6[:, 1, :], ps_z[1][:, 0:2 * P]))
                nc.vector.bn_aggr(mv[:], stats6[:]).then_inc(bn_done, 1)

            def batch_mean():
                dve.wait_ge(bn_done, 1)
                dve.wait_ge(mean_summed, 1)
                link(nc.vector.tensor_tensor(dev[:], mv[:, 0:1], ps_m[:, 0:1], ALU.subtract))
                nc.vector.scalar_tensor_tensor(out=dev2[:], in0=dev[:], scalar=dev[:], in1=mv[:, 1:2],
                                               op0=ALU.mult, op1=ALU.add).then_inc(bn_done, 1)
                nc.vector.tensor_tensor(mean_bias[:], par[:, VBIAS:VBIAS + 1], ps_m[:, 0:1],
                                        ALU.add).then_inc(bn_done, 1)
                dve.wait_ge(bn_done, 3)
                link(nc.vector.tensor_tensor(less_mean[:], par[:, VBIAS:VBIAS + 1], mean_bias[:], ALU.subtract))

            def norm_factors():
                dve.wait_ge(std_ready, 1)
                link(nc.vector.reciprocal(rstd[:], std[:]))
                link(nc.vector.tensor_tensor(gain[:], rstd[:], par[:, VGAM:VGAM + 1], ALU.mult))
                nc.vector.scalar_tensor_tensor(out=shift[:], in0=less_mean[:], scalar=gain[:],
                                               in1=par[:, VBET:VBET + 1], op0=ALU.mult,
                                               op1=ALU.add).then_inc(factors_ready, 1)
                nc.vector.tensor_tensor(scale[:], gain[:], par[:, VADD:VADD + 1], ALU.add).then_inc(factors_ready, 1)

            def find_index(c, h):
                dve.wait_ge(itag_in[c][h], 16)
                for g in range(h * G // 2, (h + 1) * G // 2):
                    last = nc.vector.max_index(idx8[:, c, g, :], ones8[:], itags[:, c, g, :])
                if h == 0:
                    return
                link(last)
                nc.vector.tensor_scalar(lohi[:, 0, c, :], idx8[:, c, :, 0], P - 1, None, ALU.bitwise_and)
                link(nc.vector.tensor_scalar(lohi[:, 1, c, :], idx8[:, c, :, 0], P.bit_length() - 1, KT - 1,
                                             ALU.logical_shift_right, ALU.bitwise_and))
                nc.vector.tensor_copy(lohi16[:, :, c, :], lohi[:, :, c, :]).then_inc(idx_ready, 1)

            def masks(c):
                n = fills.index(("index", c))
                dve.wait_ge(turned, n + 1)
                nc.vector.tensor_scalar(mask[:, c, :], ps_x[:, 0:P], par[:, VBLK:VBLK + 1], None,
                                        ALU.is_equal).then_inc(mask_ready, 1)
                nc.vector.tensor_scalar(onehot[:, c, :], ps_t[n % 4][:, :], row[:, 0:1], None,
                                        ALU.is_equal).then_inc(kept_dve, 1)

            def keep_block(c):
                dve.wait_ge(mask_ready, c + 1)
                dve.wait_ge(block_rows, c + 1)
                nc.vector.tensor_tensor(looked[:, c, :], mask[:, c, :], ps_x[:, P:2 * P],
                                        ALU.mult).then_inc(looked_ready, 1)

            def hidden1(c):
                if c == C - 1:
                    dve.wait_ge(l1_done, c + 2)
                    dst, src = h1[:, c % 2, 1, :], l1_of(c, 1)
                else:
                    dve.wait_ge(l1_done, c + 1)
                    dst, src = h1[:, c % 2].rearrange("p a n -> p (a n)"), ps_layer[:, 0:2 * P]
                dve.wait_ge(l2_done, c - 1)
                nc.vector.tensor_scalar(dst, src, par[:, VB1:VB1 + 1], 0.0, ALU.add, ALU.max).then_inc(h1_dve, 1)

            def hidden2(c):
                dve.wait_ge(l2_done, c + 1)
                dve.wait_ge(l3_done, c - 1)
                nc.vector.tensor_scalar(h2[:, c % 2, :], l2_of(c), par[:, VB2:VB2 + 1], 0.0,
                                        ALU.add, ALU.max).then_inc(h2_ready[c], 1)

            def output(c):
                dve.wait_ge(l3_done, c + 1)
                nc.vector.tensor_scalar(y[:, c, :], l3_of(c), par[0:G, VB3:VB3 + 1], 0.0,
                                        ALU.add, ALU.max).then_inc(y_ready[c], 1)

            keeps("feat")
            find_index(0, 0)
            group_statistics()
            find_index(0, 1)
            batch_mean()
            masks(0)
            norm_factors()
            keep_block(0)
            find_index(1, 0)
            find_index(1, 1)
            masks(1)
            find_index(2, 0)
            keep_block(1)
            find_index(2, 1)
            masks(2)
            find_index(3, 0)
            keep_block(2)
            find_index(3, 1)
            masks(3)
            keep_block(3)
            keeps("tag", 3)
            hidden1(2)
            hidden1(3)
            hidden2(2)
            output(2)


def _pack(i):
    p = np.zeros((P, NPACK), np.float32)
    p[:, WU:WU + DU] = i["L0_rec_W_user"].T
    p[:, WI:WI + DU] = i["L0_rec_W_item"].T
    for k in range(KT):
        p[:, EU + k * DT:EU + (k + 1) * DT] = i["L0_rec_E_item_tag"][k * P:(k + 1) * P]
        p[:, EI + k * DT:EI + (k + 1) * DT] = i["L0_rec_E_user_tag"][k * P:(k + 1) * P]
    for g in range(G):
        o = g * GW
        p[o:o + NFEAT, W1:W1 + H1] = i["L0_rec_W1"].T
        p[o:o + H2, W3:W3 + 1] = i["L0_rec_W3"].T
        p[o:o + H2, VB2] = i["L0_rec_b2"]
        for row, b, gam, bet in ((ROW_USER, "b_user", "g1", "be1"), (ROW_ITEM, "b_item", "g2", "be2")):
            p[o + row:o + row + DU, VBIAS] = i["L0_rec_" + b]
            p[o + row:o + row + DU, VGAM] = i["L0_rec_" + gam]
            p[o + row:o + row + DU, VBET] = i["L0_rec_" + bet]
        p[o + ROW_UTAG:o + ROW_UTAG + DT, VADD] = TAG_SCALE
        p[o + ROW_ITAG:o + ROW_ITAG + DT, VADD] = 1.0
    for a in range(2):
        p[a * H1:(a + 1) * H1, W2:W2 + H2] = i["L0_rec_W2"].T
        p[a * H1:(a + 1) * H1, VB1] = i["L0_rec_b1"]
    p[:, VB3] = i["L0_rec_b3"][0]
    p[:, VBLK] = np.arange(P) % GW // DT
    return p


def kernel(**inputs):
    import concourse.bacc as _bacc
    from concourse.bass_utils import run_bass_kernel_spmd as _run

    i = {k: np.asarray(v) for k, v in inputs.items()}
    arrays = {
        "user": np.ascontiguousarray(i["r_user_feature"]),
        "item": np.ascontiguousarray(i["r_item_feature"]),
        "utag": np.ascontiguousarray(i["r_user_tag"]),
        "itag": np.ascontiguousarray(i["r_item_tag"]),
        "pack": _pack(i),
    }
    nc = _bacc.Bacc("TRN2", target_bir_lowering=False, num_devices=1)
    args = [nc.dram_tensor(n, a.shape, F32, kind="ExternalInput").ap() for n, a in arrays.items()]
    out = nc.dram_tensor("out", (B, 1), F32, kind="ExternalOutput").ap()
    build(nc, *args, out)
    r = _run(nc, [arrays], core_ids=[0])
    return r.results[0]["out"]
```
